# Optimizing a Trainium2 kernel written in Bass

```python
import numpy as np
import jax
import jax.numpy as jnp

def _softmax(x, axis=-1):
    return jax.nn.softmax(x, axis=axis)
def _gelu(x):
    return jax.nn.gelu(x, approximate=True)
def _silu(x):
    return jax.nn.silu(x)
def _sigmoid(x):
    return jax.nn.sigmoid(x)
def _layernorm(x, axis=-1, eps=1e-5):
    m = jnp.mean(x, axis=axis, keepdims=True)
    v = jnp.var(x, axis=axis, keepdims=True)
    return (x - m) / jnp.sqrt(v + eps)
def _scatter_add(tgt, idx, src, axis=0):
    return tgt.at[idx].add(src)
def _segment_sum(src, seg, n):
    return jax.ops.segment_sum(src, seg, n)

kernel_name = 'mk_adj_resnorm_d1_adj_64_1c9e1d'

def setup_inputs(seed: int = 0):
    np.random.seed(seed)
    _w = jnp.asarray
    def _rec_inputs():
        import jax
        import jax.numpy as jnp
        _gk = jax.random.key(seed)
        x = -0.0001071 + 1.001 * jax.random.normal(jax.random.fold_in(_gk, 1), (8, 3000, 64), jnp.float32)
        _w = (1.0 + jnp.arange(3000, dtype=jnp.float32)) ** -0.5
        _w = _w / _w.mean()
        _pij = jnp.clip(0.00133333 * _w[:, None] * _w[None, :], 0.0, 1.0)
        _a = jax.random.uniform(jax.random.fold_in(_gk, 2), (8, 3000, 3000)) < _pij
        _af = _a.astype(jnp.float32)
        adj = _af
        return x, adj
    x, adj = _rec_inputs()
    def _L0_gnn_setup():
        import jax, jax.numpy as jnp
        import numpy as np
        B, N, F = (2, 3000, 64)
        H, OUT, ATT = (4, 16, 16)
        DENSITY = 0.01
        key = jax.random.key(seed)
        ks = jax.random.split(key, 6)
        h = jax.random.normal(ks[0], (B, N, F), dtype=jnp.float32)
        a = (jax.random.uniform(ks[1], (B, N, N)) < DENSITY).astype(jnp.float32)
        glorot = lambda k, shape: jax.random.uniform(k, shape, jnp.float32, -1.0, 1.0) * jnp.sqrt(6.0 / (shape[-2] + shape[-1]))
        kernel = glorot(ks[2], (H, F, OUT))
        attention_kernel = glorot(ks[3], (H, F, ATT))
        attention_kernel_2 = glorot(ks[4], (H, F, ATT))
        bias = jax.random.normal(ks[5], (1, 1, H, OUT), dtype=jnp.float32) * 0.01
        return {'h': h, 'a': a, 'kernel': kernel, 'attention_kernel': attention_kernel, 'attention_kernel_2': attention_kernel_2, 'bias': bias}
    _L0_gnn_all = _L0_gnn_setup()
    _L0_gnn_in = {k: v for k, v in _L0_gnn_all.items() if k in ('kernel', 'attention_kernel', 'attention_kernel_2', 'bias', )}
    del _L0_gnn_all

    return {
        "x": x,
        "adj": adj,
        "L0_gnn_kernel": _L0_gnn_in["kernel"],
        "L0_gnn_attention_kernel": _L0_gnn_in["attention_kernel"],
        "L0_gnn_attention_kernel_2": _L0_gnn_in["attention_kernel_2"],
        "L0_gnn_bias": _L0_gnn_in["bias"],
    }

def reference(x, adj, L0_gnn_kernel, L0_gnn_attention_kernel, L0_gnn_attention_kernel_2, L0_gnn_bias):
    import jax
    import jax.numpy as jnp
    def _L0_gnn_ref(h, a, kernel, attention_kernel, attention_kernel_2, bias):
        import jax, jax.numpy as jnp
        import numpy as np
        B, N, F = (2, 3000, 64)
        H, OUT, ATT = (4, 16, 16)
        DENSITY = 0.01
        feats = jnp.einsum('bnf,hfo->bhno', h, kernel)
        f_self = jnp.einsum('bnf,hfd->hbnd', h, attention_kernel)
        f_other = jnp.einsum('bnf,hfd->hbdn', h, attention_kernel_2)
        a_h = a[None]
        scores = jnp.einsum('hbnd,hbdm->hbnm', f_self, f_other)
        masked = a_h * scores
        masked = jnp.where(masked >= 0, masked, 0.2 * masked)
        masked = masked / jnp.sqrt(jnp.float32(ATT))
        masked = masked + jnp.where(a_h == 0, jnp.float32(-1000000000.0), jnp.float32(0.0))
        attn = jax.nn.softmax(masked, axis=-1)
        attn = attn * jnp.where(a_h == 0, jnp.float32(0.0), jnp.float32(1.0))
        attn = jnp.transpose(attn, (1, 0, 2, 3))
        node_features = jnp.einsum('bhnm,bhmo->bhno', attn, feats)
        node_features = node_features + jnp.transpose(bias, (0, 2, 1, 3))
        node_features = jax.nn.relu(node_features)
        node_features = jnp.transpose(node_features, (0, 2, 1, 3))
        return node_features.reshape(-1, N, H * OUT)

    x = _layernorm(x + _L0_gnn_ref(x, adj, L0_gnn_kernel, L0_gnn_attention_kernel, L0_gnn_attention_kernel_2, L0_gnn_bias), axis=-1)
    return x


_drawn_inputs = setup_inputs


def setup_inputs(seed=0):
    import zlib

    import numpy as np

    out = dict(_drawn_inputs(seed))
    spreads = {}
    factors = {'L0_gnn_bias': 8.0}
    for name, (base, spread) in spreads.items():
        noise = np.random.default_rng([zlib.crc32(name.encode()), seed]).standard_normal(out[name].shape)
        drawn = base * np.exp(spread * noise) if base else spread * noise
        out[name] = jnp.asarray(drawn.astype(out[name].dtype))
    for name, factor in factors.items():
        out[name] = (out[name] * factor).astype(out[name].dtype)
    return out
```

```python
import concourse.bass as bass
from concourse import mybir
from contextlib import ExitStack

B, N, F = 8, 3000, 64
HEADS, OUT, ATT = 4, 16, 16
ROWS = 125
TILES = N // ROWS
PAIRS = TILES // 2
ALL_TILES = B * TILES
UNITS = ALL_TILES * HEADS
SPAN = 500
GROUPS = N // (2 * SPAN)
BLOCKS = 4
STEPS = TILES // BLOCKS
LAG = 3
RELU_COLS = 1000
COPIES = 4
PENALTY = 3.0e37
FLOOR = -1.0e30
SLOPE = 0.2
EPS = 1e-5
Q_PART = (0, 1, 2, 0, 1, 2, 0, 1)
K_PART = (0, 0, 0, 1, 1, 1, 2, 2)
VW = 32


def gat_kernel(nc, x, adj, w_feat, w_self, w_other, bias, out):
    fp32, bf16 = mybir.dt.float32, mybir.dt.bfloat16
    ALU, ACT, AX = mybir.AluOpType, mybir.ActivationFunctionType, mybir.AxisListType

    x_rows = x.rearrange("b n f -> (b n) f")
    adj_rows = adj.rearrange("b n m -> (b n) m")
    out_rows = out.rearrange("b n f -> (b n) f")

    qk_dram = nc.dram_tensor("qk_parts", [B, 2, HEADS, 3, ATT, N], bf16, kind="Internal").ap()
    v_dram = nc.dram_tensor("values", [B, HEADS, ROWS, TILES * VW], fp32, kind="Internal").ap()
    qk_rows = qk_dram.rearrange("b s h t d n -> (b s h t d) n")
    HEAD_ROWS = 3 * ATT

    ctx = ExitStack()
    with ctx:
        def sb(name, shape, dt=fp32):
            return ctx.enter_context(nc.sbuf_tensor(name, shape, dt))

        def sem(name):
            return ctx.enter_context(nc.semaphore(name))

        ident = sb("ident", [128, 128])
        stack = sb("stack", [128, VW])
        w_qk = sb("w_qk", [F, 2 * HEADS * ATT])
        w_v = sb("w_v", [F, HEADS * OUT])
        bias_rows = sb("bias_rows", [ROWS, HEADS * OUT])
        minus_half = sb("minus_half", [ROWS, 1])
        parts = sb("parts", [128, 2, 3, N], bf16)
        v_prep = sb("v_prep", [ROWS, HEADS, TILES, VW])
        k_sb = sb("k_sb", [128, HEADS, N], bf16)
        v_sb = sb("v_sb", [ROWS, HEADS, TILES, VW])
        q_sb = sb("q_sb", [128, 2, HEADS, ROWS], bf16)
        pen = sb("pen", [ROWS, 2, N])
        probs = sb("probs", [128, HEADS, N])
        relu = sb("relu", [ROWS, 2, RELU_COLS])
        rest = probs[:, 0, :]
        xT = probs[0:F, 1, :]
        x_all = [probs[0:ROWS, 2 + c, 0:TILES * F].rearrange("p (t f) -> p t f", t=TILES) for c in range(2)]
        probsT = sb("probsT", [ROWS, COPIES, BLOCKS * ROWS])
        group_max = sb("group_max", [ROWS, HEADS, GROUPS])
        row_max = sb("row_max", [ROWS, HEADS])
        neg_max = sb("neg_max", [ROWS, HEADS])
        shift = sb("shift", [ROWS, HEADS])
        sums = sb("sums", [128, 2, HEADS, ROWS])
        x_in = sb("x_in", [ROWS, 2, F])
        den = sb("den", [ROWS, 2, HEADS])
        attended = sb("attended", [ROWS, 2, F])
        pre = sb("pre", [ROWS, F])
        pre2 = sb("pre2", [ROWS, 2, F])
        bn = sb("bn", [ROWS, 2, 6])
        moments = sb("moments", [ROWS, 2, 2])
        spread = sb("spread", [ROWS, 2, 2])
        y_out = sb("y_out", [ROWS, 2, F])

        bank = [ctx.enter_context(nc.psum_tensor(f"bank{i}", [128, 2 if i < 2 else 1, 512], fp32))
                for i in range(6)]
        scores_ps = [bank[0], bank[1]]
        transposed_ps = [bank[2], bank[3]]
        sums_ps = bank[4]
        final_ps = bank[5]

        const_loaded = sem("const_loaded")
        const_made = sem("const_made")
        stack_made = sem("stack_made")
        x_all_loaded = [sem(f"x_all_loaded{c}") for c in range(2)]
        prep_xT = sem("prep_xT")
        prep_xT_copied = sem("prep_xT_copied")
        prep_qk = sem("prep_qk")
        prep_first = sem("prep_first")
        prep_rest = sem("prep_rest")
        prep_second = sem("prep_second")
        prep_third = sem("prep_third")
        prep_v = sem("prep_v")
        prep_v_copied = sem("prep_v_copied")
        parts_stored = [sem(f"parts_stored{c}") for c in range(2)]
        values_stored = sem("values_stored")

        k_loaded = [sem(f"k_loaded{h}") for h in range(HEADS)]
        v_loaded = [sem(f"v_loaded{h}") for h in range(HEADS)]
        q_loaded = [sem(f"q_loaded{j}") for j in range(2)]
        adj_loaded = [sem(f"adj_loaded{j}") for j in range(2)]
        x_loaded = [sem(f"x_loaded{j}") for j in range(2)]
        out_stored = [sem(f"out_stored{j}") for j in range(2)]
        pen_ready = sem("pen_ready")
        scores_ready = sem("scores_ready")
        masked_ready = sem("masked_ready")
        dve_small = sem("dve_small")
        shift_ready = sem("shift_ready")
        leaky_ready = sem("leaky_ready")
        relu_ready = sem("relu_ready")
        added_ready = sem("added_ready")
        exp_ready = sem("exp_ready")
        transposed_ready = sem("transposed_ready")
        copied_ready = sem("copied_ready")
        weighted_done = sem("weighted_done")
        sums_copied = sem("sums_copied")
        final_ready = sem("final_ready")
        den_step = sem("den_step")
        attended_ready = sem("attended_ready")
        bn_ready = sem("bn_ready")
        moments_ready = sem("moments_ready")
        out_step = sem("out_step")
        passed = sem("passed")

        block = ctx.enter_context(nc.Block())

        def all_pairs(engine, body):
            body(0, 0, True)
            with engine.Fori(1, PAIRS) as p:
                body(0, p, False)
            with engine.Fori(1, B) as b:
                with engine.Fori(0, PAIRS) as p:
                    body(b, p, False)

        POOL_STEPS = 6
        OUT_START = 4 * POOL_STEPS
        ATTENDED_START = 1

        def all_graphs(engine, body):
            for c in range(2):
                body(c, c, c == 0)
            with engine.Fori(1, B // 2) as q:
                for c in range(2):
                    body(2 * q + c, c, False)

        def group(g):
            return slice(2 * g * SPAN, 2 * (g + 1) * SPAN)

        def alone(engine, semaphore, value):
            engine.wait_ge(semaphore, value)
            engine.sem_inc(passed, 1)

        @block.sync
        def _(sp):
            sp.dma_start(w_qk[:, 0:64].rearrange("f (h d) -> f h d", h=HEADS),
                         w_self.rearrange("h f d -> f h d")).then_inc(const_loaded, 16)
            sp.dma_start(w_qk[:, 64:128].rearrange("f (h d) -> f h d", h=HEADS),
                         w_other.rearrange("h f d -> f h d")).then_inc(const_loaded, 16)
            sp.dma_start(w_v[:, :].rearrange("f (h d) -> f h d", h=HEADS),
                         w_feat.rearrange("h f d -> f h d")).then_inc(const_loaded, 16)
            sp.dma_start(bias_rows[:, :],
                         bias.rearrange("a b h o -> (a b) (h o)").broadcast_to([ROWS, HEADS * OUT])
                         ).then_inc(const_loaded, 16)

            def load_graph(b, c, first):
                if not (isinstance(b, int) and b < 2):
                    sp.wait_ge(prep_xT, (b - 1) * STEPS)
                sp.dma_start(x_all[c], x_rows[bass.ds(b * N, N), :].rearrange("(t p) f -> p t f", p=ROWS)
                             ).then_inc(x_all_loaded[c], 16)

            def store_graph(b, c, first):
                for t, done in ((0, prep_first), (1, prep_second), (2, prep_third)):
                    sp.wait_ge(done, (b + 1) * STEPS)
                    for side in range(2):
                        sp.dma_start(qk_dram.rearrange("b s h t d n -> (b s) h t d n")
                                     [bass.ds(2 * b + side, 1), :, t, :, :].rearrange("a h d n -> (a h) d n"),
                                     parts[64 * side:64 * side + 64, c, t, :]).then_inc(parts_stored[c], 16)
                sp.wait_ge(prep_v_copied, (b + 1) * 3)
                sp.dma_start(v_dram.rearrange("b h p c -> (b h) p c")[bass.ds(b * HEADS, HEADS), :, :]
                             .rearrange("h p c -> p h c"),
                             v_prep[:, :, :, :].rearrange("p h t c -> p h (t c)")).then_inc(values_stored, 16)

            def load_adj(b, p, j, first):
                i = b * TILES + 2 * p + j
                if not first:
                    sp.wait_ge(masked_ready, (i - 1) * (HEADS * GROUPS))
                for lo, hi in ((0, 112), (112, ROWS)):
                    sp.dma_start(pen[lo:hi, j, :], adj_rows[bass.ds(i * ROWS + lo, hi - lo), :]
                                 ).then_inc(adj_loaded[j], 16)

            load_graph(0, 0, True)
            load_graph(1, 1, True)
            for j in range(2):
                load_adj(0, 0, j, True)
            store_graph(0, 0, True)
            load_graph(2, 0, False)
            store_graph(1, 1, False)
            load_graph(3, 1, False)
            with sp.Fori(1, B // 2 - 1) as q:
                for c in range(2):
                    store_graph(2 * q + c, c, False)
                    load_graph(2 * q + c + 2, c, False)
            for c in range(2):
                store_graph(B - 2 + c, c, False)
            for c in range(2):
                sp.wait_ge(parts_stored[c], B // 2 * 6 * 16)
            sp.wait_ge(values_stored, B * 16)

            def load_q(b, p, j):
                for lo, rows in ((0, 3 * ATT), (3 * ATT, 3 * ATT), (6 * ATT, 2 * ATT)):
                    sp.dma_start(q_sb[lo:lo + rows, j, :, :],
                                 qk_rows[bass.ds(b * (2 * HEADS * HEAD_ROWS), HEADS * HEAD_ROWS),
                                         bass.ds((2 * p + j) * ROWS, ROWS)]
                                 .rearrange("(h r) n -> r h n", h=HEADS)[0:rows, :, :]
                                 ).then_inc(q_loaded[j], 16)

            def load_k(b, first):
                for h in range(HEADS):
                    if not first:
                        sp.wait_ge(scores_ready, b * (TILES * HEADS * GROUPS) - (HEADS - 1 - h) * GROUPS)
                    for g in range(8):
                        sp.dma_start(k_sb[g * ATT:(g + 1) * ATT, h, :],
                                     qk_rows[bass.ds(b * (2 * HEADS * HEAD_ROWS)
                                                     + ((HEADS + h) * 3 + K_PART[g]) * ATT, ATT), :]
                                     ).then_inc(k_loaded[h], 16)

            def load_v(b, first):
                for h in range(HEADS):
                    if not first:
                        sp.wait_ge(weighted_done, b * (TILES * HEADS * STEPS) - (HEADS - 1 - h) * STEPS)
                    sp.dma_start(v_sb[:, h, :, :].rearrange("p t c -> p (t c)"),
                                 v_dram.rearrange("b h p c -> (b h p) c")
                                 [bass.ds((b * HEADS + h) * ROWS, ROWS), :]).then_inc(v_loaded[h], 16)

            def load_first_pair(b, first):
                if not first:
                    load_adj(b, 0, 0, False)
                load_q(b, 0, 0)
                load_k(b, first)
                if not first:
                    load_adj(b, 0, 1, False)
                load_q(b, 0, 1)
                load_v(b, first)

            def load_pairs(b):
                with sp.Fori(1, PAIRS) as p:
                    for j in range(2):
                        load_adj(b, p, j, False)
                        load_q(b, p, j)

            load_first_pair(0, True)
            load_pairs(0)
            with sp.Fori(1, B) as b:
                load_first_pair(b, False)
                load_pairs(b)

        @block.gpsimd
        def _(pool):
            pool.memset(ident[:, :], 0.0).then_inc(const_made, 1)
            pool.memset(minus_half[:, :], -0.5).then_inc(const_made, 1)
            pool.memset(v_prep[:, :, :, :], 0.0).then_inc(const_made, 1)
            pool.wait_ge(const_made, 3)
            pool.memset(v_prep[:, :, :, OUT:OUT + 1], 1.0).then_inc(const_made, 1)
            pool.affine_select(out=ident[:, :], in_=ident[:, :], compare_op=ALU.not_equal, fill=1.0,
                               base=0, pattern=[[-1, 128]], channel_multiplier=1).then_inc(const_made, 1)
            pool.wait_ge(const_loaded, 64)

            pool.sem_inc(out_step, OUT_START)
            for j in range(2):
                pool.dma_start(x_in[:, j, :], x_rows[j * ROWS:(j + 1) * ROWS, :]).then_inc(x_loaded[j], 16)

            def penalty(i, j, rounds):
                alone(pool, adj_loaded[j], rounds * 32)
                pool.tensor_scalar(pen[:, j, :], pen[:, j, :], -1.0, PENALTY, ALU.add, ALU.mult
                                   ).then_inc(pen_ready, 1)

            def add_relu(v, h):
                pool.wait_ge(relu_ready, v + 1)
                pool.tensor_tensor(probs[0:ROWS, h, 0:RELU_COLS], probs[0:ROWS, h, 0:RELU_COLS],
                                   relu[:, h % 2, :], ALU.add).then_inc(added_ready, 1)

            def residual(i, j, rounds, more):
                base = OUT_START + i * POOL_STEPS
                pool.wait_ge(attended_ready, i + 1 + ATTENDED_START)
                pool.wait_ge(out_step, base)
                pool.tensor_tensor(pre[:, :], attended[:, j, :], bias_rows[:, :], ALU.add).then_inc(out_step, 1)
                alone(pool, out_step, base + 1)
                pool.tensor_scalar(pre[:, :], pre[:, :], 0.0, None, ALU.max).then_inc(out_step, 1)
                pool.wait_ge(out_step, base + 2)
                pool.wait_ge(x_loaded[j], rounds * 16)
                pool.tensor_tensor(pre2[:, j, :], pre[:, :], x_in[:, j, :], ALU.add).then_inc(out_step, 1)
                pool.wait_ge(out_step, base + 3)
                if more:
                    pool.dma_start(x_in[:, j, :], x_rows[bass.ds((i + 2) * ROWS, ROWS), :]
                                   ).then_inc(x_loaded[j], 16)

            def normalised(i, j, rounds, first):
                base = OUT_START + i * POOL_STEPS
                alone(pool, moments_ready, i + 1)
                pool.tensor_scalar(spread[:, j, 0:1], moments[:, j, 1:2], EPS, None, ALU.add
                                   ).then_inc(out_step, 1)
                pool.wait_ge(out_step, base + 4)
                pool.tensor_tensor(spread[:, j, 1:2], spread[:, j, 0:1], minus_half[:, :], ALU.pow
                                   ).then_inc(out_step, 1)
                alone(pool, out_step, base + 5)
                if not first:
                    alone(pool, out_stored[j], (rounds - 1) * 16)
                pool.tensor_scalar(y_out[:, j, :], pre2[:, j, :], moments[:, j, 0:1], spread[:, j, 1:2],
                                   ALU.subtract, ALU.mult).then_inc(out_step, 1)
                pool.wait_ge(out_step, base + 6)
                pool.dma_start(out_rows[bass.ds(i * ROWS, ROWS), :], y_out[:, j, :]
                               ).then_inc(out_stored[j], 16)

            penalty(0, 0, 1)

            def pair(p, begin, end):
                for j in range(2):
                    i = 2 * p + j
                    for h in range(HEADS):
                        if not (begin and i == 0 and h == 0):
                            add_relu(i * HEADS + h - 1, (h - 1) % HEADS)
                        if h == 0 and not (begin and i < 3):
                            normalised(i - 3, 1 - j, p - 1 + j, begin and i < 5)
                        if h == 1 and not (end and j == 1):
                            penalty(i + 1, 1 - j, p + 1 + j)
                        if h == 2 and not (begin and i < 2):
                            residual(i - 2, j, p, True)

            pair(0, True, False)
            pair(1, True, False)
            pair(2, True, False)
            with pool.Fori(3, ALL_TILES // 2 - 1) as p:
                pair(p, False, False)
            pair(ALL_TILES // 2 - 1, False, True)
            add_relu(UNITS - 1, HEADS - 1)
            normalised(ALL_TILES - 3, 1, ALL_TILES // 2 - 1, False)
            for j in range(2):
                residual(ALL_TILES - 2 + j, j, ALL_TILES // 2, False)
                normalised(ALL_TILES - 2 + j, j, ALL_TILES // 2, False)
            for j in range(2):
                pool.wait_ge(out_stored[j], ALL_TILES // 2 * 16)

        @block.scalar
        def _(act):
            def project_graph(b, c, first):
                for s in range(STEPS):
                    act.wait_ge(prep_xT, b * STEPS + s + 1)
                    if s == 0 and not first:
                        act.wait_ge(prep_v, b * 3)
                        act.wait_ge(prep_qk, b * STEPS)
                    act.activation(xT[:, s * SPAN:(s + 1) * SPAN], bank[2 + s % 2][0:F, 0, 0:SPAN],
                                   ACT.Copy).then_inc(prep_xT_copied, 1)
                if not (isinstance(b, int) and b < 2):
                    act.wait_ge(parts_stored[c], (b - c) * (3 * 16))
                for s in range(STEPS + 1):
                    if s < STEPS:
                        act.wait_ge(prep_qk, b * STEPS + s + 1)
                        act.activation(parts[:, c, 0, s * SPAN:(s + 1) * SPAN],
                                       bank[s % 2][:, (s // 2) % 2, 0:SPAN], ACT.Copy).then_inc(prep_first, 1)
                    if s > 0:
                        act.wait_ge(prep_rest, b * STEPS + s)
                        act.activation(parts[:, c, 1, (s - 1) * SPAN:s * SPAN],
                                       rest[:, (s - 1) * SPAN:s * SPAN], ACT.Copy).then_inc(prep_second, 1)

            all_graphs(act, project_graph)

            def copy_step(v, hv, s):
                n = v * STEPS + s
                act.wait_ge(transposed_ready, n + 1)
                if not (isinstance(n, int) and n < COPIES):
                    act.wait_ge(weighted_done, n - COPIES + 1)
                act.activation(probsT[:, (2 * hv + s) % COPIES, :],
                               transposed_ps[s % 2][0:ROWS, 0, 0:BLOCKS * ROWS],
                               ACT.Copy).then_inc(copied_ready, 1)

            def exps(v, h, g):
                if g == 0:
                    act.wait_ge(shift_ready, v + 1)
                    act.wait_ge(leaky_ready, v + 1)
                    act.wait_ge(added_ready, v + 1)
                act.activation(probs[0:ROWS, h, group(g)], probs[0:ROWS, h, group(g)], ACT.Exp,
                               bias=shift[:, h:h + 1], scale=SLOPE / ATT ** 0.5).then_inc(exp_ready, 1)

            def relus(v, h):
                act.wait_ge(masked_ready, v * GROUPS + 1)
                if not (isinstance(v, int) and v < 2):
                    act.wait_ge(added_ready, v - 1)
                act.activation(relu[:, h % 2, :], probs[0:ROWS, h, 0:RELU_COLS], ACT.Relu,
                               scale=1.0 / SLOPE - 1.0).then_inc(relu_ready, 1)

            def copy_sums(v, h, i, j, wait):
                act.wait_ge(weighted_done, (v + 1) * STEPS)
                if wait:
                    act.wait_ge(final_ready, i - 1)
                act.activation(sums[:, 1 - j, h, :], sums_ps[:, 0, 0:ROWS], ACT.Copy).then_inc(sums_copied, 1)

            def position(u, i, j, h, wait, begin, end):
                n = u if begin else LAG + 2
                if n >= 1 and end <= 0:
                    relus(u - 1, (h - 1) % HEADS)
                for g in range(GROUPS):
                    if n >= LAG and end < LAG:
                        copy_step(u - LAG, (h - LAG) % HEADS, 2 * g)
                    if g == 0 and n >= LAG + 1:
                        copy_sums(u - LAG - 1, h, i, j, wait)
                    if n >= LAG - 1 and end < LAG - 1:
                        exps(u - LAG + 1, (h - LAG + 1) % HEADS, g)
                    if n >= LAG and end < LAG:
                        copy_step(u - LAG, (h - LAG) % HEADS, 2 * g + 1)

            def pair(b, p, first):
                for j in range(2):
                    i = b * TILES + 2 * p + j
                    for h in range(HEADS):
                        position(i * HEADS + h, i, j, h, not first, first, -1)

            all_pairs(act, pair)
            for n in range(LAG + 1):
                position(UNITS + n, ALL_TILES, 0, n, True, False, n)

        @block.vector
        def _(dve):
            dve.wait_ge(const_made, 5)
            for g in range(4):
                dve.tensor_copy(stack[32 * g:32 * g + 32, :], ident[32 * g:32 * g + 32, 32 * g:32 * g + 32]
                                ).then_inc(stack_made, 1)

            def project_graph(b, c, first):
                for s in range(STEPS + 1):
                    if s < STEPS:
                        cols = slice(s * SPAN, (s + 1) * SPAN)
                        dve.wait_ge(prep_first, b * STEPS + s + 1)
                        dve.tensor_tensor(rest[:, cols], bank[s % 2][:, (s // 2) % 2, 0:SPAN],
                                          parts[:, c, 0, cols], ALU.subtract).then_inc(prep_rest, 1)
                    if s > 0:
                        cols = slice((s - 1) * SPAN, s * SPAN)
                        dve.wait_ge(prep_second, b * STEPS + s)
                        dve.tensor_tensor(parts[:, c, 2, cols], rest[:, cols], parts[:, c, 1, cols],
                                          ALU.subtract).then_inc(prep_third, 1)
                if not first:
                    dve.wait_ge(values_stored, b * 16)
                for s in range(3):
                    dve.wait_ge(prep_v, b * 3 + s + 1)
                    dve.tensor_copy(
                        v_prep[:, :, 8 * s:8 * s + 8, 0:OUT],
                        bank[4 + s % 2][0:ROWS, 0, :].rearrange("p (t h o) -> p h t o", t=8, h=HEADS)
                    ).then_inc(prep_v_copied, 1)

            all_graphs(dve, project_graph)
            dve.sem_inc(attended_ready, ATTENDED_START)

            def masked(u, i, j, h, g, start):
                if g == 0 and h == 0:
                    dve.wait_ge(pen_ready, i + 1)
                if not start:
                    dve.wait_ge(transposed_ready, (u - HEADS) * STEPS + 2 * g + 2)
                alone(dve, scores_ready, u * GROUPS + g + 1)
                dve.tensor_tensor_reduce(
                    out=probs[0:ROWS, h, group(g)].rearrange("p (a c) -> p a c", a=2),
                    in0=scores_ps[(h * GROUPS + g) % 2][0:ROWS, :, 0:SPAN],
                    in1=pen[:, j, group(g)].rearrange("p (a c) -> p a c", a=2),
                    scale=1.0, scalar=FLOOR, op0=ALU.add, op1=ALU.max,
                    accum_out=group_max[:, h, g:g + 1]).then_inc(masked_ready, 1)

            def leaky(h, lo, hi):
                return dve.scalar_tensor_tensor(
                    out=probs[0:ROWS, h, lo:hi], in0=probs[0:ROWS, h, lo:hi], scalar=1.0 / SLOPE,
                    in1=probs[0:ROWS, h, lo:hi], op0=ALU.mult, op1=ALU.max)

            def last_leaky(v, h):
                leaky(h, 2 * (GROUPS - 1) * SPAN, N).then_inc(leaky_ready, 1)
                dve.wait_ge(dve_small, 2 * v + 1)
                dve.tensor_scalar(neg_max[:, h:h + 1], row_max[:, h:h + 1], -1.0 / ATT ** 0.5, None,
                                  ALU.mult).then_inc(dve_small, 1)

            def row_shift(v, h, start):
                dve.wait_ge(dve_small, 2 * v + 2)
                if not start:
                    dve.wait_ge(exp_ready, (v - HEADS + 1) * GROUPS)
                dve.scalar_tensor_tensor(out=shift[:, h:h + 1], in0=neg_max[:, h:h + 1], scalar=SLOPE,
                                         in1=neg_max[:, h:h + 1], op0=ALU.mult, op1=ALU.min
                                         ).then_inc(shift_ready, 1)

            def unit(u, i, j, h, start):
                before = not (start and h == 0)
                v, hv = u - 1, (h - 1) % HEADS
                masked(u, i, j, h, 0, start)
                if before:
                    last_leaky(v, hv)
                masked(u, i, j, h, 1, start)
                if before:
                    row_shift(v, hv, isinstance(v, int) and v < HEADS)
                masked(u, i, j, h, 2, start)
                dve.wait_ge(masked_ready, u * GROUPS + 2)
                leaky(h, RELU_COLS, 2 * (GROUPS - 1) * SPAN)
                dve.wait_ge(masked_ready, (u + 1) * GROUPS)
                dve.reduce_max(row_max[:, h:h + 1], group_max[:, h, :], AX.X).then_inc(dve_small, 1)

            def normalise(i, j, first):
                dve.wait_ge(final_ready, i + 2)
                if not first:
                    dve.wait_ge(out_step, OUT_START + (i - 2) * POOL_STEPS + 1)
                dve.tensor_scalar(den[:, j, :], final_ps[0:ROWS, 0, 0:HEADS * VW]
                                  .rearrange("p (h c) -> p h c", h=HEADS)[:, :, OUT], 1e-30, None, ALU.max
                                  ).then_inc(den_step, 1)
                dve.wait_ge(den_step, 2 * i + 1)
                dve.reciprocal(den[:, j, :], den[:, j, :]).then_inc(den_step, 1)
                dve.wait_ge(den_step, 2 * i + 2)
                dve.tensor_tensor(
                    attended[:, j, :].rearrange("p (h o) -> p h o", h=HEADS),
                    final_ps[0:ROWS, 0, 0:HEADS * VW].rearrange("p (h c) -> p h c", h=HEADS)[:, :, 0:OUT],
                    den[:, j, :].unsqueeze(2).broadcast_to([ROWS, HEADS, OUT]), ALU.mult
                ).then_inc(attended_ready, 1)

            def statistics(i, j):
                dve.wait_ge(out_step, OUT_START + i * POOL_STEPS + 3)
                dve.bn_stats(bn[:, j, :], pre2[:, j, :]).then_inc(bn_ready, 1)
                alone(dve, bn_ready, i + 1)
                dve.bn_aggr(moments[:, j, :], bn[:, j, :]).then_inc(moments_ready, 1)

            def pair(b, p, first):
                for j in range(2):
                    i = b * TILES + 2 * p + j
                    for h in range(HEADS):
                        unit(i * HEADS + h, i, j, h, first and j == 0)
                        if h == 0 and not first:
                            normalise(i - 2, j, False)
                        if h == HEADS - 1 and not first:
                            statistics(i - 2, j)

            all_pairs(dve, pair)
            last_leaky(UNITS - 1, HEADS - 1)
            row_shift(UNITS - 1, HEADS - 1, False)
            for j in range(2):
                normalise(ALL_TILES - 2 + j, j, False)
                statistics(ALL_TILES - 2 + j, j)

        @block.tensor
        def _(pe):
            pe.wait_ge(const_made, 5)
            pe.wait_ge(const_loaded, 64)

            def project_graph(b, c, first):
                alone(pe, x_all_loaded[c], (b - c) * 8 + 16)
                for s in range(STEPS):
                    if not (first and s < 2):
                        alone(pe, prep_xT_copied, b * STEPS + s - 1)
                    for t in range(BLOCKS):
                        last = pe.transpose(bank[2 + s % 2][0:F, 0, t * ROWS:(t + 1) * ROWS],
                                            x_all[c][:, s * BLOCKS + t, :], ident[0:ROWS, 0:ROWS])
                    last.then_inc(prep_xT, 1)
                for s in range(STEPS):
                    pe.wait_ge(prep_xT_copied, b * STEPS + s + 1)
                    if not (first and s < 4):
                        pe.wait_ge(prep_rest, b * STEPS + s - 3)
                        pe.wait_ge(prep_first, b * STEPS + s - 3)
                    pe.matmul(bank[s % 2][:, (s // 2) % 2, 0:SPAN], w_qk[:, :],
                              xT[:, s * SPAN:(s + 1) * SPAN], start=True, stop=True).then_inc(prep_qk, 1)
                for s in range(3):
                    if not (first and s < 2):
                        pe.wait_ge(prep_v_copied, b * 3 + s - 1)
                    for t in range(8):
                        last = pe.matmul(bank[4 + s % 2][0:ROWS, 0, t * 64:(t + 1) * 64],
                                         xT[:, (8 * s + t) * ROWS:(8 * s + t + 1) * ROWS], w_v[:, :],
                                         start=True, stop=True)
                    last.then_inc(prep_v, 1)

            all_graphs(pe, project_graph)
            pe.wait_ge(prep_v_copied, B * 3)
            pe.wait_ge(prep_rest, B * STEPS)
            pe.wait_ge(stack_made, 4)
            pe.sem_inc(final_ready, 1)

            def scores(u, j, h, g, b, start):
                n = u * GROUPS + g
                if g == 0:
                    pe.wait_ge(k_loaded[h], (b + 1) * (8 * 16))
                if not (start and n < 2):
                    pe.wait_ge(masked_ready, n - 1)
                for c in range(2):
                    lo = (2 * g + c) * SPAN
                    last = pe.matmul(scores_ps[(h * GROUPS + g) % 2][0:ROWS, c, 0:SPAN],
                                     q_sb[:, j, h, :], k_sb[:, h, lo:lo + SPAN], start=True, stop=True)
                last.then_inc(scores_ready, 1)

            def transposes(v, h, s):
                n = v * STEPS + s
                if s % 2 == 0:
                    pe.wait_ge(exp_ready, v * GROUPS + s // 2 + 1)
                if not (isinstance(n, int) and n < 2):
                    pe.wait_ge(copied_ready, n - 1)
                for c in range(BLOCKS):
                    m = (s * BLOCKS + c) * ROWS
                    last = pe.transpose(transposed_ps[s % 2][0:ROWS, 0, c * ROWS:(c + 1) * ROWS],
                                        probs[0:ROWS, h, m:m + ROWS], ident[0:ROWS, 0:ROWS])
                last.then_inc(transposed_ready, 1)

            def weighted(v, h, s, b):
                n = v * STEPS + s
                if s == 0:
                    if b is not None:
                        pe.wait_ge(v_loaded[h], (b + 1) * 16)
                    if not (isinstance(v, int) and v < 1):
                        pe.wait_ge(sums_copied, v)
                pe.wait_ge(copied_ready, n + 1)
                buf = (2 * h + s) % COPIES
                for c in range(BLOCKS):
                    last = pe.matmul(sums_ps[32 * c:32 * c + VW, 0, 0:ROWS], v_sb[:, h, s * BLOCKS + c, :],
                                     probsT[:, buf, c * ROWS:(c + 1) * ROWS],
                                     start=(s == 0), stop=(s == STEPS - 1), tile_position=(0, 32 * c))
                last.then_inc(weighted_done, 1)

            def final(i, j, first):
                pe.wait_ge(sums_copied, (i + 1) * HEADS)
                if not first:
                    pe.wait_ge(attended_ready, i + ATTENDED_START)
                for h in range(HEADS):
                    last = pe.matmul(final_ps[0:ROWS, 0, h * VW:(h + 1) * VW], sums[:, j, h, :], stack[:, :],
                                     start=True, stop=True)
                last.then_inc(final_ready, 1)

            def lagged(v, h, k, b, before):
                transposes(v, h, k)
                if k > 0:
                    weighted(v, h, k - 1, b)
                elif before:
                    weighted(v - 1, (h - 1) % HEADS, STEPS - 1, b)

            def pair(b, p, first):
                for j in range(2):
                    i = b * TILES + 2 * p + j
                    start = first and j == 0
                    pe.wait_ge(q_loaded[j], (b * PAIRS + p + 1) * (3 * 16))
                    for h in range(HEADS):
                        u = i * HEADS + h
                        for g in range(GROUPS):
                            scores(u, j, h, g, b, start and h == 0)
                            if h == 0 and g == 0 and not first:
                                final(i - 2, j, False)
                            if start and h < LAG:
                                continue
                            for k in (2 * g, 2 * g + 1):
                                lagged(u - LAG, (h - LAG) % HEADS, k, b if h >= LAG or j == 1 else None,
                                       not (start and h == LAG))

            all_pairs(pe, pair)
            final(ALL_TILES - 2, 0, False)
            for v in range(UNITS - LAG, UNITS):
                for k in range(STEPS):
                    lagged(v, v % HEADS, k, None, True)
            weighted(UNITS - 1, HEADS - 1, STEPS - 1, None)
            final(ALL_TILES - 1, 1, False)


_INS = ["x", "adj", "L0_gnn_kernel", "L0_gnn_attention_kernel", "L0_gnn_attention_kernel_2", "L0_gnn_bias"]


def kernel(**inputs):
    import numpy as _np
    import concourse.bacc as _bacc
    from concourse import mybir as _mybir
    from concourse.bass_utils import run_bass_kernel_spmd as _run

    nc = _bacc.Bacc("TRN2", target_bir_lowering=False, num_devices=1)
    arrays, args = {}, []
    for name in _INS:
        a = _np.ascontiguousarray(inputs[name])
        arrays[f"in_{name}"] = a
        args.append(nc.dram_tensor(f"in_{name}", a.shape, _mybir.dt.from_np(a.dtype), kind="ExternalInput").ap())
    out = nc.dram_tensor("out_0", (B, N, F), _mybir.dt.from_np(_np.dtype("float32")), kind="ExternalOutput").ap()
    gat_kernel(nc, *args, out)
    r = _run(nc, [arrays], core_ids=[0])
    return r.results[0]["out_0"]
```

```python
import concourse.bass as bass
from concourse import mybir
from contextlib import ExitStack

B, N, F = 8, 3000, 64
HEADS, OUT, ATT = 4, 16, 16
ROWS = 125
TILES = N // ROWS
PAIRS = TILES // 2
ALL_TILES = B * TILES
UNITS = ALL_TILES * HEADS
SPAN = 500
GROUPS = N // (2 * SPAN)
BLOCKS = 4
STEPS = TILES // BLOCKS
EXPS = 3
LAG = 3
POOL_COLS = 1900
COPIES = 4
PENALTY = 3.0e37
FLOOR = -1.0e30
SLOPE = 0.2
EPS = 1e-5
Q_PART = (0, 1, 2, 0, 1, 2, 0, 1)
K_PART = (0, 0, 0, 1, 1, 1, 2, 2)
VW = 32


def gat_kernel(nc, x, adj, w_feat, w_self, w_other, bias, out):
    fp32, bf16 = mybir.dt.float32, mybir.dt.bfloat16
    ALU, ACT, AX = mybir.AluOpType, mybir.ActivationFunctionType, mybir.AxisListType

    x_rows = x.rearrange("b n f -> (b n) f")
    adj_rows = adj.rearrange("b n m -> (b n) m")
    out_rows = out.rearrange("b n f -> (b n) f")

    qk_dram = nc.dram_tensor("qk_parts", [B, 2, HEADS, 3, ATT, N], bf16, kind="Internal").ap()
    v_dram = nc.dram_tensor("values", [B, HEADS, ROWS, TILES * VW], fp32, kind="Internal").ap()
    qk_rows = qk_dram.rearrange("b s h t d n -> (b s h t d) n")
    HEAD_ROWS = 3 * ATT

    ctx = ExitStack()
    with ctx:
        def sb(name, shape, dt=fp32):
            return ctx.enter_context(nc.sbuf_tensor(name, shape, dt))

        def sem(name):
            return ctx.enter_context(nc.semaphore(name))

        ident = sb("ident", [128, 128])
        stack = sb("stack", [128, VW])
        w_qk = sb("w_qk", [F, 2 * HEADS * ATT])
        w_v = sb("w_v", [F, HEADS * OUT])
        bias_rows = sb("bias_rows", [ROWS, HEADS * OUT])
        minus_half = sb("minus_half", [ROWS, 1])
        parts = sb("parts", [128, 2, 3, N], bf16)
        v_prep = sb("v_prep", [ROWS, HEADS, TILES, VW])
        k_sb = sb("k_sb", [128, HEADS, N], bf16)
        v_sb = sb("v_sb", [ROWS, HEADS, TILES, VW])
        q_sb = sb("q_sb", [128, 2, HEADS, ROWS], bf16)
        pen = sb("pen", [ROWS, 2, N])
        probs = sb("probs", [128, HEADS, N])
        relu = sb("relu", [ROWS, 2, POOL_COLS])
        rest = probs[:, 0, :]
        xT_odd = sb("xT_odd", [F, N])
        xT = [probs[0:F, 1, :], xT_odd[:, :]]
        x_all = [probs[0:ROWS, 2 + c, 0:TILES * F].rearrange("p (t f) -> p t f", t=TILES) for c in range(2)]
        probsT = sb("probsT", [ROWS, COPIES, BLOCKS * ROWS])
        group_max = sb("group_max", [ROWS, HEADS, GROUPS])
        row_max = sb("row_max", [ROWS, HEADS])
        neg_max = sb("neg_max", [ROWS, HEADS])
        shift = sb("shift", [ROWS, HEADS])
        sums = sb("sums", [128, 2, HEADS, ROWS])
        x_in = sb("x_in", [ROWS, 2, F])
        den = sb("den", [ROWS, 2, HEADS])
        attended = sb("attended", [ROWS, 2, F])
        pre = sb("pre", [ROWS, F])
        pre2 = sb("pre2", [ROWS, 2, F])
        bn = sb("bn", [ROWS, 2, 6])
        moments = sb("moments", [ROWS, 2, 2])
        spread = sb("spread", [ROWS, 2, 2])
        y_out = sb("y_out", [ROWS, 2, F])

        bank = [ctx.enter_context(nc.psum_tensor(f"bank{i}", [128, 2 if i < 2 else 1, 512], fp32))
                for i in range(6)]
        scores_ps = [bank[0], bank[1]]
        transposed_ps = [bank[2], bank[3]]
        sums_ps = bank[4]
        final_ps = bank[5]

        const_loaded = sem("const_loaded")
        const_made = sem("const_made")
        stack_made = sem("stack_made")
        x_all_loaded = [sem(f"x_all_loaded{c}") for c in range(2)]
        prep_xT = sem("prep_xT")
        prep_xT_copied = sem("prep_xT_copied")
        prep_qk = sem("prep_qk")
        prep_first = sem("prep_first")
        prep_rest = sem("prep_rest")
        prep_second = sem("prep_second")
        prep_third = sem("prep_third")
        prep_v = sem("prep_v")
        prep_v_copied = sem("prep_v_copied")
        parts_stored = [sem(f"parts_stored{c}") for c in range(2)]
        values_stored = sem("values_stored")

        k_loaded = [sem(f"k_loaded{h}") for h in range(HEADS)]
        v_loaded = [sem(f"v_loaded{h}") for h in range(HEADS)]
        q_loaded = [sem(f"q_loaded{j}") for j in range(2)]
        adj_loaded = [sem(f"adj_loaded{j}") for j in range(2)]
        x_loaded = [sem(f"x_loaded{j}") for j in range(2)]
        out_stored = [sem(f"out_stored{j}") for j in range(2)]
        pen_ready = sem("pen_ready")
        scores_ready = sem("scores_ready")
        masked_ready = sem("masked_ready")
        dve_small = sem("dve_small")
        shift_ready = sem("shift_ready")
        leaky_ready = sem("leaky_ready")
        relu_ready = sem("relu_ready")
        added_ready = sem("added_ready")
        exp_ready = sem("exp_ready")
        transposed_ready = sem("transposed_ready")
        copied_ready = sem("copied_ready")
        weighted_done = sem("weighted_done")
        sums_copied = sem("sums_copied")
        final_ready = sem("final_ready")
        den_step = sem("den_step")
        attended_ready = sem("attended_ready")
        bn_ready = sem("bn_ready")
        moments_ready = sem("moments_ready")
        out_step = sem("out_step")
        passed = sem("passed")

        block = ctx.enter_context(nc.Block())

        def all_pairs(engine, body):
            body(0, 0, True)
            with engine.Fori(1, PAIRS) as p:
                body(0, p, False)
            with engine.Fori(1, B) as b:
                with engine.Fori(0, PAIRS) as p:
                    body(b, p, False)

        POOL_STEPS = 6
        OUT_START = 4 * POOL_STEPS
        ATTENDED_START = 1

        def all_graphs(engine, body):
            for c in range(2):
                body(c, c, c == 0)
            with engine.Fori(1, B // 2) as q:
                for c in range(2):
                    body(2 * q + c, c, False)

        def group(g):
            return slice(2 * g * SPAN, 2 * (g + 1) * SPAN)

        def alone(engine, semaphore, value):
            engine.wait_ge(semaphore, value)
            engine.sem_inc(passed, 1)

        @block.sync
        def _(sp):
            sp.dma_start(w_qk[:, 0:64].rearrange("f (h d) -> f h d", h=HEADS),
                         w_self.rearrange("h f d -> f h d")).then_inc(const_loaded, 16)
            sp.dma_start(w_qk[:, 64:128].rearrange("f (h d) -> f h d", h=HEADS),
                         w_other.rearrange("h f d -> f h d")).then_inc(const_loaded, 16)
            sp.dma_start(w_v[:, :].rearrange("f (h d) -> f h d", h=HEADS),
                         w_feat.rearrange("h f d -> f h d")).then_inc(const_loaded, 16)
            sp.dma_start(bias_rows[:, :],
                         bias.rearrange("a b h o -> (a b) (h o)").broadcast_to([ROWS, HEADS * OUT])
                         ).then_inc(const_loaded, 16)

            def load_graph(b, c, first):
                if not (isinstance(b, int) and b < 2):
                    sp.wait_ge(prep_xT, (b - 1) * STEPS)
                sp.dma_start(x_all[c], x_rows[bass.ds(b * N, N), :].rearrange("(t p) f -> p t f", p=ROWS)
                             ).then_inc(x_all_loaded[c], 16)

            def store_graph(b, c, first):
                for t, done in ((0, prep_first), (1, prep_second), (2, prep_third)):
                    sp.wait_ge(done, (b + 1) * STEPS)
                    for side in range(2):
                        sp.dma_start(qk_dram.rearrange("b s h t d n -> (b s) h t d n")
                                     [bass.ds(2 * b + side, 1), :, t, :, :].rearrange("a h d n -> (a h) d n"),
                                     parts[64 * side:64 * side + 64, c, t, :]).then_inc(parts_stored[c], 16)
                sp.wait_ge(prep_v_copied, (b + 1) * 3)
                sp.dma_start(v_dram.rearrange("b h p c -> (b h) p c")[bass.ds(b * HEADS, HEADS), :, :]
                             .rearrange("h p c -> p h c"),
                             v_prep[:, :, :, :].rearrange("p h t c -> p h (t c)")).then_inc(values_stored, 16)

            def load_adj(b, p, j, first):
                i = b * TILES + 2 * p + j
                if not first:
                    sp.wait_ge(masked_ready, (i - 1) * (HEADS * GROUPS))
                for lo, hi in ((0, 112), (112, ROWS)):
                    sp.dma_start(pen[lo:hi, j, :], adj_rows[bass.ds(i * ROWS + lo, hi - lo), :]
                                 ).then_inc(adj_loaded[j], 16)

            load_graph(0, 0, True)
            load_graph(1, 1, True)
            for j in range(2):
                load_adj(0, 0, j, True)
            store_graph(0, 0, True)
            load_graph(2, 0, False)
            store_graph(1, 1, False)
            load_graph(3, 1, False)
            with sp.Fori(1, B // 2 - 1) as q:
                for c in range(2):
                    store_graph(2 * q + c, c, False)
                    load_graph(2 * q + c + 2, c, False)
            store_graph(B - 2, 0, False)
            sp.wait_ge(parts_stored[0], B // 2 * 6 * 16)
            sp.wait_ge(values_stored, (B - 1) * 16)

            def load_q(b, p, j):
                for lo, rows in ((0, 3 * ATT), (3 * ATT, 3 * ATT), (6 * ATT, 2 * ATT)):
                    sp.dma_start(q_sb[lo:lo + rows, j, :, :],
                                 qk_rows[bass.ds(b * (2 * HEADS * HEAD_ROWS), HEADS * HEAD_ROWS),
                                         bass.ds((2 * p + j) * ROWS, ROWS)]
                                 .rearrange("(h r) n -> r h n", h=HEADS)[0:rows, :, :]
                                 ).then_inc(q_loaded[j], 16)

            def load_k(b, first):
                for h in range(HEADS):
                    if not first:
                        sp.wait_ge(scores_ready, b * (TILES * HEADS * GROUPS) - (HEADS - 1 - h) * GROUPS)
                    for g in range(8):
                        sp.dma_start(k_sb[g * ATT:(g + 1) * ATT, h, :],
                                     qk_rows[bass.ds(b * (2 * HEADS * HEAD_ROWS)
                                                     + ((HEADS + h) * 3 + K_PART[g]) * ATT, ATT), :]
                                     ).then_inc(k_loaded[h], 16)

            def load_v(b, first):
                for h in range(HEADS):
                    if not first:
                        sp.wait_ge(weighted_done, b * (TILES * HEADS * STEPS) - (HEADS - 1 - h) * STEPS)
                    sp.dma_start(v_sb[:, h, :, :].rearrange("p t c -> p (t c)"),
                                 v_dram.rearrange("b h p c -> (b h p) c")
                                 [bass.ds((b * HEADS + h) * ROWS, ROWS), :]).then_inc(v_loaded[h], 16)

            def load_first_pair(b, first):
                if not first:
                    load_adj(b, 0, 0, False)
                load_q(b, 0, 0)
                load_k(b, first)
                if not first:
                    load_adj(b, 0, 1, False)
                load_q(b, 0, 1)
                load_v(b, first)

            def load_pairs(b):
                with sp.Fori(1, PAIRS) as p:
                    for j in range(2):
                        load_adj(b, p, j, False)
                        load_q(b, p, j)

            load_first_pair(0, True)
            store_graph(B - 1, 1, False)
            sp.wait_ge(parts_stored[1], B // 2 * 6 * 16)
            sp.wait_ge(values_stored, B * 16)
            load_pairs(0)
            with sp.Fori(1, B) as b:
                load_first_pair(b, False)
                load_pairs(b)

        @block.gpsimd
        def _(pool):
            pool.memset(ident[:, :], 0.0).then_inc(const_made, 1)
            pool.memset(minus_half[:, :], -0.5).then_inc(const_made, 1)
            pool.memset(v_prep[:, :, :, :], 0.0).then_inc(const_made, 1)
            pool.wait_ge(const_made, 3)
            pool.memset(v_prep[:, :, :, OUT:OUT + 1], 1.0).then_inc(const_made, 1)
            pool.affine_select(out=ident[:, :], in_=ident[:, :], compare_op=ALU.not_equal, fill=1.0,
                               base=0, pattern=[[-1, 128]], channel_multiplier=1).then_inc(const_made, 1)
            pool.wait_ge(const_loaded, 64)

            pool.sem_inc(out_step, OUT_START)
            for j in range(2):
                pool.dma_start(x_in[:, j, :], x_rows[j * ROWS:(j + 1) * ROWS, :]).then_inc(x_loaded[j], 16)

            def penalty(i, j, rounds):
                alone(pool, adj_loaded[j], rounds * 32)
                pool.tensor_scalar(pen[:, j, :], pen[:, j, :], -1.0, PENALTY, ALU.add, ALU.mult
                                   ).then_inc(pen_ready, 1)

            def add_relu(v, h):
                pool.wait_ge(relu_ready, v + 1)
                pool.tensor_tensor(probs[0:ROWS, h, 0:POOL_COLS], probs[0:ROWS, h, 0:POOL_COLS],
                                   relu[:, h % 2, :], ALU.add).then_inc(added_ready, 1)

            def residual(i, j, rounds, more):
                base = OUT_START + i * POOL_STEPS
                pool.wait_ge(attended_ready, i + 1 + ATTENDED_START)
                pool.wait_ge(out_step, base)
                pool.tensor_tensor(pre[:, :], attended[:, j, :], bias_rows[:, :], ALU.add).then_inc(out_step, 1)
                alone(pool, out_step, base + 1)
                pool.tensor_scalar(pre[:, :], pre[:, :], 0.0, None, ALU.max).then_inc(out_step, 1)
                pool.wait_ge(out_step, base + 2)
                pool.wait_ge(x_loaded[j], rounds * 16)
                pool.tensor_tensor(pre2[:, j, :], pre[:, :], x_in[:, j, :], ALU.add).then_inc(out_step, 1)
                pool.wait_ge(out_step, base + 3)
                if more:
                    pool.dma_start(x_in[:, j, :], x_rows[bass.ds((i + 2) * ROWS, ROWS), :]
                                   ).then_inc(x_loaded[j], 16)

            def normalised(i, j, rounds, first):
                base = OUT_START + i * POOL_STEPS
                alone(pool, moments_ready, i + 1)
                pool.tensor_scalar(spread[:, j, 0:1], moments[:, j, 1:2], EPS, None, ALU.add
                                   ).then_inc(out_step, 1)
                pool.wait_ge(out_step, base + 4)
                pool.tensor_tensor(spread[:, j, 1:2], spread[:, j, 0:1], minus_half[:, :], ALU.pow
                                   ).then_inc(out_step, 1)
                alone(pool, out_step, base + 5)
                if not first:
                    alone(pool, out_stored[j], (rounds - 1) * 16)
                pool.tensor_scalar(y_out[:, j, :], pre2[:, j, :], moments[:, j, 0:1], spread[:, j, 1:2],
                                   ALU.subtract, ALU.mult).then_inc(out_step, 1)
                pool.wait_ge(out_step, base + 6)
                pool.dma_start(out_rows[bass.ds(i * ROWS, ROWS), :], y_out[:, j, :]
                               ).then_inc(out_stored[j], 16)

            penalty(0, 0, 1)

            def pair(p, begin, end):
                for j in range(2):
                    i = 2 * p + j
                    for h in range(HEADS):
                        if not (begin and i == 0 and h == 0):
                            add_relu(i * HEADS + h - 1, (h - 1) % HEADS)
                        if h == 0 and not (begin and i < 3):
                            normalised(i - 3, 1 - j, p - 1 + j, begin and i < 5)
                        if h == 1 and not (end and j == 1):
                            penalty(i + 1, 1 - j, p + 1 + j)
                        if h == 2 and not (begin and i < 2):
                            residual(i - 2, j, p, True)

            pair(0, True, False)
            pair(1, True, False)
            pair(2, True, False)
            with pool.Fori(3, ALL_TILES // 2 - 1) as p:
                pair(p, False, False)
            pair(ALL_TILES // 2 - 1, False, True)
            add_relu(UNITS - 1, HEADS - 1)
            normalised(ALL_TILES - 3, 1, ALL_TILES // 2 - 1, False)
            for j in range(2):
                residual(ALL_TILES - 2 + j, j, ALL_TILES // 2, False)
                normalised(ALL_TILES - 2 + j, j, ALL_TILES // 2, False)
            for j in range(2):
                pool.wait_ge(out_stored[j], ALL_TILES // 2 * 16)

        @block.scalar
        def _(act):
            def project_graph(b, c, first):
                for s in range(STEPS):
                    act.wait_ge(prep_xT, b * STEPS + s + 1)
                    if s == 0 and not (isinstance(b, int) and b < 2):
                        act.wait_ge(prep_v, (b - 1) * 3)
                        act.wait_ge(prep_qk, (b - 1) * STEPS)
                    act.activation(xT[c][:, s * SPAN:(s + 1) * SPAN], bank[2 + s % 2][0:F, 0, 0:SPAN],
                                   ACT.Copy).then_inc(prep_xT_copied, 1)
                if not (isinstance(b, int) and b < 2):
                    act.wait_ge(parts_stored[c], (b - c) * (3 * 16))
                for s in range(STEPS + 1):
                    if s < STEPS:
                        act.wait_ge(prep_qk, b * STEPS + s + 1)
                        act.activation(parts[:, c, 0, s * SPAN:(s + 1) * SPAN],
                                       bank[s % 2][:, (s // 2) % 2, 0:SPAN], ACT.Copy).then_inc(prep_first, 1)
                    if s > 0:
                        act.wait_ge(prep_rest, b * STEPS + s)
                        act.activation(parts[:, c, 1, (s - 1) * SPAN:s * SPAN],
                                       rest[:, (s - 1) * SPAN:s * SPAN], ACT.Copy).then_inc(prep_second, 1)

            all_graphs(act, project_graph)

            def copy_step(v, hv, s):
                n = v * STEPS + s
                act.wait_ge(transposed_ready, n + 1)
                if not (isinstance(n, int) and n < COPIES):
                    act.wait_ge(weighted_done, n - COPIES + 1)
                act.activation(probsT[:, (2 * hv + s) % COPIES, :],
                               transposed_ps[s % 2][0:ROWS, 0, 0:BLOCKS * ROWS],
                               ACT.Copy).then_inc(copied_ready, 1)

            def exps(v, h, g):
                cols = slice(g * (N // EXPS), (g + 1) * (N // EXPS))
                if g == 0:
                    act.wait_ge(shift_ready, v + 1)
                    act.wait_ge(leaky_ready, v + 1)
                    act.wait_ge(added_ready, v + 1)
                act.activation(probs[0:ROWS, h, cols], probs[0:ROWS, h, cols], ACT.Exp,
                               bias=shift[:, h:h + 1], scale=SLOPE / ATT ** 0.5).then_inc(exp_ready, 1)

            def copy_sums(v, h, i, j, wait):
                act.wait_ge(weighted_done, (v + 1) * STEPS)
                if wait:
                    act.wait_ge(final_ready, i - 1)
                act.activation(sums[:, 1 - j, h, :], sums_ps[:, 0, 0:ROWS], ACT.Copy).then_inc(sums_copied, 1)

            ORDER = "CSECCECCEC"

            def position(u, i, j, h, wait, begin, end):
                n = u if begin else LAG + 2
                e = c = 0
                for what in ORDER:
                    if what == "C":
                        if n >= LAG and end < LAG:
                            copy_step(u - LAG, (h - LAG) % HEADS, c)
                        c += 1
                    elif what == "S":
                        if n >= LAG + 1:
                            copy_sums(u - LAG - 1, h, i, j, wait)
                    else:
                        if n >= LAG - 1 and end < LAG - 1:
                            exps(u - LAG + 1, (h - LAG + 1) % HEADS, e)
                        e += 1

            def pair(b, p, first):
                for j in range(2):
                    i = b * TILES + 2 * p + j
                    for h in range(HEADS):
                        position(i * HEADS + h, i, j, h, not first, first, -1)

            all_pairs(act, pair)
            for n in range(LAG + 1):
                position(UNITS + n, ALL_TILES, 0, n, True, False, n)

        @block.vector
        def _(dve):
            dve.wait_ge(const_made, 5)
            for g in range(4):
                dve.tensor_copy(stack[32 * g:32 * g + 32, :], ident[32 * g:32 * g + 32, 32 * g:32 * g + 32]
                                ).then_inc(stack_made, 1)

            def project_graph(b, c, first):
                for s in range(STEPS + 1):
                    if s < STEPS:
                        cols = slice(s * SPAN, (s + 1) * SPAN)
                        dve.wait_ge(prep_first, b * STEPS + s + 1)
                        dve.tensor_tensor(rest[:, cols], bank[s % 2][:, (s // 2) % 2, 0:SPAN],
                                          parts[:, c, 0, cols], ALU.subtract).then_inc(prep_rest, 1)
                    if s > 0:
                        cols = slice((s - 1) * SPAN, s * SPAN)
                        dve.wait_ge(prep_second, b * STEPS + s)
                        dve.tensor_tensor(parts[:, c, 2, cols], rest[:, cols], parts[:, c, 1, cols],
                                          ALU.subtract).then_inc(prep_third, 1)
                if not first:
                    dve.wait_ge(values_stored, b * 16)
                for s in range(3):
                    dve.wait_ge(prep_v, b * 3 + s + 1)
                    dve.tensor_copy(
                        v_prep[:, :, 8 * s:8 * s + 8, 0:OUT],
                        bank[4 + s % 2][0:ROWS, 0, :].rearrange("p (t h o) -> p h t o", t=8, h=HEADS)
                    ).then_inc(prep_v_copied, 1)

            all_graphs(dve, project_graph)
            dve.sem_inc(attended_ready, ATTENDED_START)

            def masked(u, i, j, h, g, start):
                if g == 0 and h == 0:
                    dve.wait_ge(pen_ready, i + 1)
                if not start:
                    dve.wait_ge(transposed_ready, (u - HEADS) * STEPS + 2 * g + 2)
                alone(dve, scores_ready, u * GROUPS + g + 1)
                dve.tensor_tensor_reduce(
                    out=probs[0:ROWS, h, group(g)].rearrange("p (a c) -> p a c", a=2),
                    in0=scores_ps[(h * GROUPS + g) % 2][0:ROWS, :, 0:SPAN],
                    in1=pen[:, j, group(g)].rearrange("p (a c) -> p a c", a=2),
                    scale=1.0, scalar=FLOOR, op0=ALU.add, op1=ALU.max,
                    accum_out=group_max[:, h, g:g + 1]).then_inc(masked_ready, 1)

            def leaky(h, lo, hi):
                return dve.scalar_tensor_tensor(
                    out=probs[0:ROWS, h, lo:hi], in0=probs[0:ROWS, h, lo:hi], scalar=1.0 / SLOPE,
                    in1=probs[0:ROWS, h, lo:hi], op0=ALU.mult, op1=ALU.max)

            def last_leaky(v, h):
                dve.wait_ge(masked_ready, (v + 1) * GROUPS)
                leaky(h, POOL_COLS, N).then_inc(leaky_ready, 1)
                dve.reduce_max(row_max[:, h:h + 1], group_max[:, h, :], AX.X).then_inc(dve_small, 1)

            def negate(v, h):
                dve.wait_ge(dve_small, 2 * v + 1)
                dve.tensor_scalar(neg_max[:, h:h + 1], row_max[:, h:h + 1], -1.0 / ATT ** 0.5, None,
                                  ALU.mult).then_inc(dve_small, 1)

            def row_shift(v, h, start):
                dve.wait_ge(dve_small, 2 * v + 2)
                if not start:
                    dve.wait_ge(exp_ready, (v - HEADS + 1) * EXPS)
                dve.scalar_tensor_tensor(out=shift[:, h:h + 1], in0=neg_max[:, h:h + 1], scalar=SLOPE,
                                         in1=neg_max[:, h:h + 1], op0=ALU.mult, op1=ALU.min
                                         ).then_inc(shift_ready, 1)

            def unit(u, i, j, h, start):
                before = not (start and h == 0)
                v, hv = u - 1, (h - 1) % HEADS
                masked(u, i, j, h, 0, start)
                if before:
                    last_leaky(v, hv)
                masked(u, i, j, h, 1, start)
                if before:
                    negate(v, hv)
                masked(u, i, j, h, 2, start)
                if before:
                    row_shift(v, hv, isinstance(v, int) and v < HEADS)
                if not (isinstance(u, int) and u < 2):
                    dve.wait_ge(added_ready, u - 1)
                dve.wait_ge(masked_ready, u * GROUPS + 2)
                dve.tensor_scalar(relu[:, h % 2, :], probs[0:ROWS, h, 0:POOL_COLS], 0.0,
                                  1.0 / SLOPE - 1.0, ALU.max, ALU.mult).then_inc(relu_ready, 1)

            def normalise(i, j, first):
                dve.wait_ge(final_ready, i + 2)
                if not first:
                    dve.wait_ge(out_step, OUT_START + (i - 2) * POOL_STEPS + 1)
                dve.tensor_scalar(den[:, j, :], final_ps[0:ROWS, 0, 0:HEADS * VW]
                                  .rearrange("p (h c) -> p h c", h=HEADS)[:, :, OUT], 1e-30, None, ALU.max
                                  ).then_inc(den_step, 1)
                dve.wait_ge(den_step, 2 * i + 1)
                dve.reciprocal(den[:, j, :], den[:, j, :]).then_inc(den_step, 1)
                dve.wait_ge(den_step, 2 * i + 2)
                dve.tensor_tensor(
                    attended[:, j, :].rearrange("p (h o) -> p h o", h=HEADS),
                    final_ps[0:ROWS, 0, 0:HEADS * VW].rearrange("p (h c) -> p h c", h=HEADS)[:, :, 0:OUT],
                    den[:, j, :].unsqueeze(2).broadcast_to([ROWS, HEADS, OUT]), ALU.mult
                ).then_inc(attended_ready, 1)

            def statistics(i, j):
                dve.wait_ge(out_step, OUT_START + i * POOL_STEPS + 3)
                dve.bn_stats(bn[:, j, :], pre2[:, j, :]).then_inc(bn_ready, 1)
                alone(dve, bn_ready, i + 1)
                dve.bn_aggr(moments[:, j, :], bn[:, j, :]).then_inc(moments_ready, 1)

            def pair(b, p, first):
                for j in range(2):
                    i = b * TILES + 2 * p + j
                    for h in range(HEADS):
                        unit(i * HEADS + h, i, j, h, first and j == 0)
                        if h == 0 and not first:
                            normalise(i - 2, j, False)
                        if h == HEADS - 1 and not first:
                            statistics(i - 2, j)

            all_pairs(dve, pair)
            last_leaky(UNITS - 1, HEADS - 1)
            negate(UNITS - 1, HEADS - 1)
            row_shift(UNITS - 1, HEADS - 1, False)
            for j in range(2):
                normalise(ALL_TILES - 2 + j, j, False)
                statistics(ALL_TILES - 2 + j, j)

        @block.tensor
        def _(pe):
            pe.wait_ge(const_made, 5)
            pe.wait_ge(const_loaded, 64)

            def project_graph(b, c, first):
                alone(pe, x_all_loaded[c], (b - c) * 8 + 16)
                for s in range(STEPS):
                    if not (first and s < 2):
                        alone(pe, prep_xT_copied, b * STEPS + s - 1)
                    for t in range(BLOCKS):
                        last = pe.transpose(bank[2 + s % 2][0:F, 0, t * ROWS:(t + 1) * ROWS],
                                            x_all[c][:, s * BLOCKS + t, :], ident[0:ROWS, 0:ROWS])
                    last.then_inc(prep_xT, 1)
                for s in range(STEPS):
                    pe.wait_ge(prep_xT_copied, b * STEPS + s + 1)
                    if not (first and s < 4):
                        pe.wait_ge(prep_rest, b * STEPS + s - 3)
                        pe.wait_ge(prep_first, b * STEPS + s - 3)
                    pe.matmul(bank[s % 2][:, (s // 2) % 2, 0:SPAN], w_qk[:, :],
                              xT[c][:, s * SPAN:(s + 1) * SPAN], start=True, stop=True).then_inc(prep_qk, 1)
                for s in range(3):
                    if not (first and s < 2):
                        pe.wait_ge(prep_v_copied, b * 3 + s - 1)
                    for t in range(8):
                        last = pe.matmul(bank[4 + s % 2][0:ROWS, 0, t * 64:(t + 1) * 64],
                                         xT[c][:, (8 * s + t) * ROWS:(8 * s + t + 1) * ROWS], w_v[:, :],
                                         start=True, stop=True)
                    last.then_inc(prep_v, 1)

            all_graphs(pe, project_graph)
            pe.wait_ge(prep_v_copied, B * 3)
            pe.wait_ge(prep_rest, B * STEPS)
            pe.wait_ge(stack_made, 4)
            pe.sem_inc(final_ready, 1)

            def scores(u, j, h, g, b, start):
                n = u * GROUPS + g
                if g == 0:
                    pe.wait_ge(k_loaded[h], (b + 1) * (8 * 16))
                if not (start and n < 2):
                    pe.wait_ge(masked_ready, n - 1)
                for c in range(2):
                    lo = (2 * g + c) * SPAN
                    last = pe.matmul(scores_ps[(h * GROUPS + g) % 2][0:ROWS, c, 0:SPAN],
                                     q_sb[:, j, h, :], k_sb[:, h, lo:lo + SPAN], start=True, stop=True)
                last.then_inc(scores_ready, 1)

            def transposes(v, h, s):
                n = v * STEPS + s
                if s * EXPS % STEPS == 0:
                    pe.wait_ge(exp_ready, v * EXPS + s * EXPS // STEPS + 1)
                if not (isinstance(n, int) and n < 2):
                    pe.wait_ge(copied_ready, n - 1)
                for c in range(BLOCKS):
                    m = (s * BLOCKS + c) * ROWS
                    last = pe.transpose(transposed_ps[s % 2][0:ROWS, 0, c * ROWS:(c + 1) * ROWS],
                                        probs[0:ROWS, h, m:m + ROWS], ident[0:ROWS, 0:ROWS])
                last.then_inc(transposed_ready, 1)

            def weighted(v, h, s, b):
                n = v * STEPS + s
                if s == 0:
                    if b is not None:
                        pe.wait_ge(v_loaded[h], (b + 1) * 16)
                    if not (isinstance(v, int) and v < 1):
                        pe.wait_ge(sums_copied, v)
                pe.wait_ge(copied_ready, n + 1)
                buf = (2 * h + s) % COPIES
                for c in range(BLOCKS):
                    last = pe.matmul(sums_ps[32 * c:32 * c + VW, 0, 0:ROWS], v_sb[:, h, s * BLOCKS + c, :],
                                     probsT[:, buf, c * ROWS:(c + 1) * ROWS],
                                     start=(s == 0), stop=(s == STEPS - 1), tile_position=(0, 32 * c))
                last.then_inc(weighted_done, 1)

            def final(i, j, h, v):
                pe.wait_ge(sums_copied, v + 1)
                if h == 0 and not (isinstance(i, int) and i < 1):
                    pe.wait_ge(attended_ready, i + ATTENDED_START)
                done = pe.matmul(final_ps[0:ROWS, 0, h * VW:(h + 1) * VW],
                                 sums[:, j, h, :], stack[:, :], start=True, stop=True)
                if h == HEADS - 1:
                    done.then_inc(final_ready, 1)

            ORDER = "TSWTWTSWTWTSWTFW"

            def interleaved(u, tile, j, h, b, b_values, start):
                v, hv = u - LAG, (h - LAG) % HEADS
                lagged = not (start and h < LAG)
                g = t = 0
                w = -1
                for what in ORDER:
                    if what == "S":
                        scores(u, j, h, g, b, start and h == 0)
                        g += 1
                    elif what == "T":
                        if lagged:
                            transposes(v, hv, t)
                        t += 1
                    elif what == "F":
                        if h > 0 and not start:
                            for k in ((h - 1,) if h < HEADS - 1 else (h - 1, h)):
                                final(tile - 1, 1 - j, k, u - HEADS - h + k)
                    else:
                        if lagged and w >= 0:
                            weighted(v, hv, w, b_values)
                        elif lagged and not (start and h == LAG):
                            weighted(v - 1, (hv - 1) % HEADS, STEPS - 1, b_values)
                        w += 1

            def trailing(v, h):
                for s in range(STEPS):
                    transposes(v, h, s)
                    if s > 0:
                        weighted(v, h, s - 1, None)
                    else:
                        weighted(v - 1, (h - 1) % HEADS, STEPS - 1, None)

            def pair(b, p, first):
                for j in range(2):
                    i = b * TILES + 2 * p + j
                    start = first and j == 0
                    pe.wait_ge(q_loaded[j], (b * PAIRS + p + 1) * (3 * 16))
                    for h in range(HEADS):
                        u = i * HEADS + h
                        interleaved(u, i, j, h, b, b if h >= LAG or j == 1 else None, start)

            all_pairs(pe, pair)
            for v in range(UNITS - LAG, UNITS):
                trailing(v, v % HEADS)
            weighted(UNITS - 1, HEADS - 1, STEPS - 1, None)
            for h in range(HEADS):
                final(ALL_TILES - 1, 1, h, UNITS - HEADS + h)


_INS = ["x", "adj", "L0_gnn_kernel", "L0_gnn_attention_kernel", "L0_gnn_attention_kernel_2", "L0_gnn_bias"]


def kernel(**inputs):
    import numpy as _np
    import concourse.bacc as _bacc
    from concourse import mybir as _mybir
    from concourse.bass_utils import run_bass_kernel_spmd as _run

    nc = _bacc.Bacc("TRN2", target_bir_lowering=False, num_devices=1)
    arrays, args = {}, []
    for name in _INS:
        a = _np.ascontiguousarray(inputs[name])
        arrays[f"in_{name}"] = a
        args.append(nc.dram_tensor(f"in_{name}", a.shape, _mybir.dt.from_np(a.dtype), kind="ExternalInput").ap())
    out = nc.dram_tensor("out_0", (B, N, F), _mybir.dt.from_np(_np.dtype("float32")), kind="ExternalOutput").ap()
    gat_kernel(nc, *args, out)
    r = _run(nc, [arrays], core_ids=[0])
    return r.results[0]["out_0"]
```
